# Optimizing a Trainium2 kernel written in Bass

```python
import numpy as np
import jax
import jax.numpy as jnp

def _softmax(x, axis=-1):
    return jax.nn.softmax(x, axis=axis)

def _gelu(x):
    return jax.nn.gelu(x, approximate=True)

def _silu(x):
    return jax.nn.silu(x)

def _sigmoid(x):
    return jax.nn.sigmoid(x)

def _layernorm(x, axis=-1, eps=1e-05):
    m = jnp.mean(x, axis=axis, keepdims=True)
    v = jnp.var(x, axis=axis, keepdims=True)
    return (x - m) / jnp.sqrt(v + eps)

def _scatter_add(tgt, idx, src, axis=0):
    return tgt.at[idx].add(src)

def _segment_sum(src, seg, n):
    return jax.ops.segment_sum(src, seg, n)
kernel_name = 'mk_gnn_resnorm_d2_gnn_r8_bd3a6d'

def setup_inputs(seed: int=0):
    np.random.seed(seed)
    _w = jnp.asarray

    def _rec_inputs():
        import jax
        import jax.numpy as jnp
        _gk = jax.random.key(seed)
        x = -0.0005121 + 1.001 * jax.random.normal(jax.random.fold_in(_gk, 1), (12500, 32), jnp.float32)
        src = jax.random.randint(jax.random.fold_in(_gk, 2), (400000,), 0, 12500, jnp.int32)
        dst = jnp.minimum((12500 * jax.random.uniform(jax.random.fold_in(_gk, 3), (400000,)) ** 2.0).astype(jnp.int32), 99999)
        _o = jnp.argsort(dst, stable=True)
        src = src[_o]
        dst = dst[_o]
        edge_attr_2 = jax.random.uniform(jax.random.fold_in(_gk, 11), (400000, 2), jnp.float32, 0.0, 1)
        edge_attr_3 = 0.000844983 + 0.999762 * jax.random.normal(jax.random.fold_in(_gk, 12), (400000, 3), jnp.float32)
        edge_weight = jax.random.uniform(jax.random.fold_in(_gk, 14), (400000,), jnp.float32, 0.0, 1)
        return (x, src, dst, edge_attr_2, edge_attr_3, edge_weight)
    x, src, dst, edge_attr_2, edge_attr_3, edge_weight = _rec_inputs()

    def _L0_gnn_setup():
        import jax, jax.numpy as jnp
        import numpy as np
        N_NODES = 12500
        N_EDGES = 400000
        IN_CH = 32
        OUT_CH = 32
        DIM = 2
        KSIZE = 3

        def _basis(pseudo):
            p = jnp.clip(pseudo, 0.0, 1.0)
            grid = jnp.linspace(0.0, 1.0, KSIZE, dtype=p.dtype)
            dist = jnp.abs(p[:, :, None] - grid[None, None, :])
            b = jnp.maximum(1.0 - dist * (KSIZE - 1), 0.0)
            basis = jnp.einsum('ea,eb->eab', b[:, 0], b[:, 1])
            return basis.reshape(p.shape[0], -1)
        key = jax.random.key(seed)
        k1, k2, k3, k4, k5, k6 = jax.random.split(key, 6)
        x = jax.random.normal(k1, (N_NODES, IN_CH), dtype=jnp.float32)
        pseudo = jax.random.uniform(k2, (N_EDGES, DIM), dtype=jnp.float32)
        weight = jax.random.normal(k3, (KSIZE * KSIZE, IN_CH, OUT_CH), dtype=jnp.float32) / np.sqrt(IN_CH)
        root_w = jax.random.normal(k4, (OUT_CH, IN_CH), dtype=jnp.float32) / np.sqrt(IN_CH)
        root_b = jax.random.normal(k5, (OUT_CH,), dtype=jnp.float32) * 0.01
        edge_index = jax.random.randint(k6, (2, N_EDGES), 0, N_NODES, dtype=jnp.int64)
        return {'x': x, 'pseudo': pseudo, 'weight': weight, 'root_w': root_w, 'root_b': root_b, 'edge_index': edge_index}
    _L0_gnn_all = _L0_gnn_setup()
    _L0_gnn_in = {k: v for k, v in _L0_gnn_all.items() if k in ('weight', 'root_w', 'root_b')}
    del _L0_gnn_all

    def _L1_gnn_setup():
        import jax, jax.numpy as jnp
        import numpy as np
        from math import factorial, pi, sqrt
        MUL = 8
        RS = [(MUL, 0), (MUL, 1)]
        N_NODES = 2500
        N_EDGES = 80000
        FEAT_DIM = sum((m * (2 * l + 1) for m, l in RS))
        R_DIM = sum((mo * mi * (2 * min(lo, li) + 1) for mo, lo in RS for mi, li in RS))
        HIDDEN = 64

        def _cg(j1, j2, j3, m1, m2, m3):
            if m1 + m2 != m3:
                return 0.0
            f = factorial
            pre = sqrt((2 * j3 + 1) * f(j3 + j1 - j2) * f(j3 - j1 + j2) * f(j1 + j2 - j3) / f(j1 + j2 + j3 + 1))
            pre *= sqrt(f(j3 + m3) * f(j3 - m3) * f(j1 - m1) * f(j1 + m1) * f(j2 - m2) * f(j2 + m2))
            kmin = max(0, j2 - j3 - m1, j1 - j3 + m2)
            kmax = min(j1 + j2 - j3, j1 - m1, j2 + m2)
            s = 0.0
            for k in range(kmin, kmax + 1):
                s += (-1) ** k / (f(k) * f(j1 + j2 - j3 - k) * f(j1 - m1 - k) * f(j2 + m2 - k) * f(j3 - j2 + m1 + k) * f(j3 - j1 - m2 + k))
            return pre * s

        def _w3j_complex(l1, l2, l3):
            w = np.zeros((2 * l1 + 1, 2 * l2 + 1, 2 * l3 + 1))
            for m1 in range(-l1, l1 + 1):
                for m2 in range(-l2, l2 + 1):
                    m3 = -(m1 + m2)
                    if abs(m3) <= l3:
                        w[m1 + l1, m2 + l2, m3 + l3] = (-1) ** (l1 - l2 - m3) / sqrt(2 * l3 + 1) * _cg(l1, l2, l3, m1, m2, -m3)
            return w

        def _A(l):
            A = np.zeros((2 * l + 1, 2 * l + 1), dtype=complex)
            A[l, l] = 1.0
            for m in range(1, l + 1):
                A[l + m, l + m] = (-1) ** m / sqrt(2)
                A[l + m, l - m] = 1.0 / sqrt(2)
                A[l - m, l - m] = 1j / sqrt(2)
                A[l - m, l + m] = -1j * (-1) ** m / sqrt(2)
            return A

        def real_w3j(l1, l2, l3):
            wc = _w3j_complex(l1, l2, l3).astype(complex)
            wr = np.einsum('abc,ma,nb,oc->mno', wc, _A(l1).conj(), _A(l2).conj(), _A(l3).conj())
            i = int(np.argmax(np.abs(wr)))
            ph = wr.flat[i] / abs(wr.flat[i])
            wr = wr / ph
            assert np.abs(wr.imag).max() < 1e-10
            return np.real(wr).astype(np.float32)
        _W3J = {}
        for _mo, _lo in RS:
            for _mi, _li in RS:
                for _lf in range(abs(_lo - _li), _lo + _li + 1):
                    if (_lo, _lf, _li) not in _W3J:
                        _W3J[_lo, _lf, _li] = jnp.asarray(real_w3j(_lo, _lf, _li))
        _NORM = []
        for _mo, _lo in RS:
            _num = sum((mi * (2 * min(_lo, li) + 1) for mi, li in RS))
            _NORM.append(sqrt(4.0 * pi) * sqrt(2.0 * _lo + 1.0) / sqrt(_num))
        _F_OFFS = [0] + list(np.cumsum([mi * (2 * li + 1) for mi, li in RS]))

        def spherical_harmonics(rel_vec):
            r = rel_vec / jnp.linalg.norm(rel_vec, axis=-1, keepdims=True)
            x, y, z = (r[:, 0], r[:, 1], r[:, 2])
            y0 = jnp.full_like(x, 0.5 / sqrt(pi))[:, None]
            c1 = sqrt(3.0 / (4.0 * pi))
            y1 = c1 * jnp.stack([y, z, x], axis=-1)
            c2a = 0.5 * sqrt(15.0 / pi)
            c2b = 0.25 * sqrt(5.0 / pi)
            c2c = 0.25 * sqrt(15.0 / pi)
            y2 = jnp.stack([c2a * x * y, c2a * y * z, c2b * (3.0 * z * z - 1.0), c2a * x * z, c2c * (x * x - y * y)], axis=-1)
            return jnp.concatenate([y0, y1, y2], axis=-1)
        key = jax.random.key(seed)
        ks = jax.random.split(key, 6)
        features = jax.random.normal(ks[0], (N_NODES, FEAT_DIM), dtype=jnp.float32)
        abs_distances = jax.random.uniform(ks[1], (N_EDGES,), dtype=jnp.float32, minval=0.1, maxval=1.0)
        rel_vec = jax.random.normal(ks[2], (N_EDGES, 3), dtype=jnp.float32)
        edge_index = jax.random.randint(ks[3], (2, N_EDGES), 0, N_NODES, dtype=jnp.int32)
        w1 = jax.random.normal(ks[4], (1, HIDDEN), dtype=jnp.float32)
        b1 = jnp.zeros((HIDDEN,), jnp.float32)
        w2 = jax.random.normal(ks[5], (HIDDEN, R_DIM), dtype=jnp.float32) / sqrt(HIDDEN)
        b2 = jnp.zeros((R_DIM,), jnp.float32)
        return {'features': features, 'abs_distances': abs_distances, 'rel_vec': rel_vec, 'edge_index': edge_index, 'w1': w1, 'b1': b1, 'w2': w2, 'b2': b2}
    _L1_gnn_all = _L1_gnn_setup()
    _L1_gnn_in = {k: v for k, v in _L1_gnn_all.items() if k in ('w1', 'b1', 'w2', 'b2')}
    del _L1_gnn_all
    return {'x': x, 'src': src, 'dst': dst, 'edge_attr_2': edge_attr_2, 'edge_attr_3': edge_attr_3, 'edge_weight': edge_weight, 'L0_gnn_weight': _L0_gnn_in['weight'], 'L0_gnn_root_w': _L0_gnn_in['root_w'], 'L0_gnn_root_b': _L0_gnn_in['root_b'], 'L1_gnn_w1': _L1_gnn_in['w1'], 'L1_gnn_b1': _L1_gnn_in['b1'], 'L1_gnn_w2': _L1_gnn_in['w2'], 'L1_gnn_b2': _L1_gnn_in['b2']}

def reference(x, src, dst, edge_attr_2, edge_attr_3, edge_weight, L0_gnn_weight, L0_gnn_root_w, L0_gnn_root_b, L1_gnn_w1, L1_gnn_b1, L1_gnn_w2, L1_gnn_b2):
    import jax
    import jax.numpy as jnp

    def _L0_gnn_ref(x, pseudo, weight, root_w, root_b, edge_index):
        import jax, jax.numpy as jnp
        import numpy as np
        N_NODES = 12500
        N_EDGES = 400000
        IN_CH = 32
        OUT_CH = 32
        DIM = 2
        KSIZE = 3

        def _basis(pseudo):
            p = jnp.clip(pseudo, 0.0, 1.0)
            grid = jnp.linspace(0.0, 1.0, KSIZE, dtype=p.dtype)
            dist = jnp.abs(p[:, :, None] - grid[None, None, :])
            b = jnp.maximum(1.0 - dist * (KSIZE - 1), 0.0)
            basis = jnp.einsum('ea,eb->eab', b[:, 0], b[:, 1])
            return basis.reshape(p.shape[0], -1)
        row, col = (edge_index[0], edge_index[1])
        basis = _basis(pseudo)
        messages = jnp.einsum('ek,ei,kio->eo', basis, x[row], weight)
        out = jnp.zeros((x.shape[0], weight.shape[2]), dtype=x.dtype).at[col].add(messages)
        degree = jnp.zeros((x.shape[0],), dtype=x.dtype).at[col].add(jnp.ones_like(col, dtype=x.dtype))
        out = out / jnp.maximum(degree, 1.0)[:, None]
        out = out + x @ root_w.T + root_b
        return out

    def _L1_gnn_ref(features, abs_distances, rel_vec, edge_index, w1, b1, w2, b2):
        import jax, jax.numpy as jnp
        import numpy as np
        from math import factorial, pi, sqrt
        MUL = 8
        RS = [(MUL, 0), (MUL, 1)]
        N_NODES = 2500
        N_EDGES = 80000
        FEAT_DIM = sum((m * (2 * l + 1) for m, l in RS))
        R_DIM = sum((mo * mi * (2 * min(lo, li) + 1) for mo, lo in RS for mi, li in RS))
        HIDDEN = 64

        def _cg(j1, j2, j3, m1, m2, m3):
            if m1 + m2 != m3:
                return 0.0
            f = factorial
            pre = sqrt((2 * j3 + 1) * f(j3 + j1 - j2) * f(j3 - j1 + j2) * f(j1 + j2 - j3) / f(j1 + j2 + j3 + 1))
            pre *= sqrt(f(j3 + m3) * f(j3 - m3) * f(j1 - m1) * f(j1 + m1) * f(j2 - m2) * f(j2 + m2))
            kmin = max(0, j2 - j3 - m1, j1 - j3 + m2)
            kmax = min(j1 + j2 - j3, j1 - m1, j2 + m2)
            s = 0.0
            for k in range(kmin, kmax + 1):
                s += (-1) ** k / (f(k) * f(j1 + j2 - j3 - k) * f(j1 - m1 - k) * f(j2 + m2 - k) * f(j3 - j2 + m1 + k) * f(j3 - j1 - m2 + k))
            return pre * s

        def _w3j_complex(l1, l2, l3):
            w = np.zeros((2 * l1 + 1, 2 * l2 + 1, 2 * l3 + 1))
            for m1 in range(-l1, l1 + 1):
                for m2 in range(-l2, l2 + 1):
                    m3 = -(m1 + m2)
                    if abs(m3) <= l3:
                        w[m1 + l1, m2 + l2, m3 + l3] = (-1) ** (l1 - l2 - m3) / sqrt(2 * l3 + 1) * _cg(l1, l2, l3, m1, m2, -m3)
            return w

        def _A(l):
            A = np.zeros((2 * l + 1, 2 * l + 1), dtype=complex)
            A[l, l] = 1.0
            for m in range(1, l + 1):
                A[l + m, l + m] = (-1) ** m / sqrt(2)
                A[l + m, l - m] = 1.0 / sqrt(2)
                A[l - m, l - m] = 1j / sqrt(2)
                A[l - m, l + m] = -1j * (-1) ** m / sqrt(2)
            return A

        def real_w3j(l1, l2, l3):
            wc = _w3j_complex(l1, l2, l3).astype(complex)
            wr = np.einsum('abc,ma,nb,oc->mno', wc, _A(l1).conj(), _A(l2).conj(), _A(l3).conj())
            i = int(np.argmax(np.abs(wr)))
            ph = wr.flat[i] / abs(wr.flat[i])
            wr = wr / ph
            assert np.abs(wr.imag).max() < 1e-10
            return np.real(wr).astype(np.float32)
        _W3J = {}
        for _mo, _lo in RS:
            for _mi, _li in RS:
                for _lf in range(abs(_lo - _li), _lo + _li + 1):
                    if (_lo, _lf, _li) not in _W3J:
                        _W3J[_lo, _lf, _li] = jnp.asarray(real_w3j(_lo, _lf, _li))
        _NORM = []
        for _mo, _lo in RS:
            _num = sum((mi * (2 * min(_lo, li) + 1) for mi, li in RS))
            _NORM.append(sqrt(4.0 * pi) * sqrt(2.0 * _lo + 1.0) / sqrt(_num))
        _F_OFFS = [0] + list(np.cumsum([mi * (2 * li + 1) for mi, li in RS]))

        def spherical_harmonics(rel_vec):
            r = rel_vec / jnp.linalg.norm(rel_vec, axis=-1, keepdims=True)
            x, y, z = (r[:, 0], r[:, 1], r[:, 2])
            y0 = jnp.full_like(x, 0.5 / sqrt(pi))[:, None]
            c1 = sqrt(3.0 / (4.0 * pi))
            y1 = c1 * jnp.stack([y, z, x], axis=-1)
            c2a = 0.5 * sqrt(15.0 / pi)
            c2b = 0.25 * sqrt(5.0 / pi)
            c2c = 0.25 * sqrt(15.0 / pi)
            y2 = jnp.stack([c2a * x * y, c2a * y * z, c2b * (3.0 * z * z - 1.0), c2a * x * z, c2c * (x * x - y * y)], axis=-1)
            return jnp.concatenate([y0, y1, y2], axis=-1)
        src, dst = (edge_index[0], edge_index[1])
        R = jax.nn.relu(abs_distances[:, None] @ w1 + b1) @ w2 + b2
        Y = spherical_harmonics(rel_vec)
        Fj = features[src]
        E = Fj.shape[0]
        msg_blocks = []
        r_off = 0
        for i, (mo, lo) in enumerate(RS):
            acc = jnp.zeros((E, mo, 2 * lo + 1), dtype=features.dtype)
            for j, (mi, li) in enumerate(RS):
                n_lf = 2 * min(lo, li) + 1
                sz = mo * mi * n_lf
                Rb = R[:, r_off:r_off + sz].reshape(E, mo, mi, n_lf)
                r_off += sz
                Fb = Fj[:, _F_OFFS[j]:_F_OFFS[j + 1]].reshape(E, mi, 2 * li + 1)
                for k, lf in enumerate(range(abs(lo - li), lo + li + 1)):
                    C = _W3J[lo, lf, li]
                    Yf = Y[:, lf * lf:(lf + 1) * (lf + 1)]
                    acc = acc + _NORM[i] * jnp.einsum('euv,ef,evi,ofi->euo', Rb[..., k], Yf, Fb, C)
            msg_blocks.append(acc.reshape(E, -1))
        msg = jnp.concatenate(msg_blocks, axis=-1)
        out = jnp.zeros((features.shape[0], msg.shape[1]), dtype=features.dtype)
        out = out.at[dst].add(msg)
        return out
    edge_index = jnp.stack([src, dst])
    x = _layernorm(x + _L0_gnn_ref(x, edge_attr_2, L0_gnn_weight, L0_gnn_root_w, L0_gnn_root_b, edge_index), axis=-1)
    x = _layernorm(x + _L1_gnn_ref(x, edge_weight, edge_attr_3, edge_index, L1_gnn_w1, L1_gnn_b1, L1_gnn_w2, L1_gnn_b2), axis=-1)
    return x

_drawn_inputs = setup_inputs


def setup_inputs(seed=0):
    import zlib

    import numpy as np

    out = dict(_drawn_inputs(seed))
    spreads = {'L1_gnn_b1': (0.0, 0.1), 'L1_gnn_b2': (0.0, 0.1)}
    factors = {}
    for name, (base, spread) in spreads.items():
        noise = np.random.default_rng([zlib.crc32(name.encode()), seed]).standard_normal(out[name].shape)
        drawn = base * np.exp(spread * noise) if base else spread * noise
        out[name] = jnp.asarray(drawn.astype(out[name].dtype))
    for name, factor in factors.items():
        out[name] = (out[name] * factor).astype(out[name].dtype)
    return out
```

```python
from contextlib import ExitStack

import concourse.bass as bass
from concourse import mybir

ALU = mybir.AluOpType
ACT = mybir.ActivationFunctionType
F32 = mybir.dt.float32
I32 = mybir.dt.int32
AX_X = mybir.AxisListType.X

P = 128
N = 12500
E = 400000
C = 32
T = E // P
G = 5
U = 5
B = T // (G * U)
TPP = 25
PL = T // TPP
WINDOW = 64
NP, NJ = 125, 100
TW = 8
HID = 64
R = 384
MUL = 8
ROW = 96
EPS = 1e-5
SLOTS = 3
CREDIT = U

SLOT = [u % SLOTS for u in range(U)]
AGO = [u - max(w for w in range(u - U, u) if SLOT[w % U] == SLOT[u]) for u in range(U)]


def place(g, u):
    return (g, u) if u < U else (g + 1, u - U)


def done(g, u):
    return g * U + (u + 1)


def freed(g, u):
    return g * U + (u - AGO[u] + 1 + CREDIT)


def filled(g, u, each):
    same = [w for w in range(U) if SLOT[w] == SLOT[u]]
    return g * (len(same) * each) + (same.index(u) + 1) * each


def build_program(nc, x, src, dst, edge_attr_2, edge_attr_3, edge_weight, weight0, root_w, root_b,
                  w1, b1, w2, b2, out):
    spans_dram = nc.dram_tensor("spans_dram", (PL, TW), F32).ap()
    table_dram = nc.dram_tensor("table_dram", (N, ROW), F32).ap()
    with ExitStack() as whole:
        def sbuf(name, shape, dtype=F32, scope=whole):
            return scope.enter_context(nc.sbuf_tensor(name, shape, dtype))

        keep = {
            "acc": sbuf("acc", [P, 12800]),
            "src_t": sbuf("src_t", [P, T], I32),
            "rel_t": sbuf("rel_t", [P, T]),
            "edge_t": sbuf("edge_t", [P, T * 6]),
            "nodes": sbuf("nodes", [P, NJ * C]),
            "ident": sbuf("ident", [P, P]),
            "iota": sbuf("iota", [P, WINDOW]),
            "window": sbuf("window", [P, WINDOW]),
            "base_f": sbuf("base_f", [P, B * TW]),
            "base_now": sbuf("base_now", [1, B * TW]),
            "base_i": sbuf("base_i", [1, B * TW], I32),
            "span_i": sbuf("span_i", [1, 1], I32),
        }
        prepare_edges(nc, keep, x, src, dst, edge_attr_2, spans_dram)
        spline_edges(nc, keep, x, weight0)
        spline_nodes(nc, keep, root_w, root_b, edge_attr_3, table_dram)
        tensor_edges(nc, keep, table_dram, edge_weight, w1, b1, w2, b2)
        tensor_nodes(nc, keep, out)


def prepare_edges(nc, keep, x, src, dst, edge_attr_2, spans_dram):
    acc, edge_t, ident, nodes = keep["acc"], keep["edge_t"], keep["ident"], keep["nodes"]
    src_t, rel_t, base_f = keep["src_t"], keep["rel_t"], keep["base_f"]
    raw = TPP * P
    with ExitStack() as ctx:
        def sbuf(name, shape, dtype=F32):
            return ctx.enter_context(nc.sbuf_tensor(name, shape, dtype))

        def sem(name):
            return ctx.enter_context(nc.semaphore(name))

        dst_f, src_f, attr = acc[0:PL, 0:raw], acc[0:PL, raw:2 * raw], acc[0:PL, 2 * raw:4 * raw]
        dst_i = edge_t[0:PL, 0:raw].bitcast(I32)
        src_i = edge_t[0:PL, raw:2 * raw].bitcast(I32)
        low = sbuf("low", [PL, TPP])
        high = sbuf("high", [PL, TPP])
        span5 = sbuf("span5", [PL, U])
        spans = sbuf("spans", [PL, TW])
        widest = sbuf("widest", [1, 1])
        pos = sbuf("pos", [P, 2, T])
        turn = [ctx.enter_context(nc.psum_tensor(f"turn{n}", [P, 4, P], F32)) for n in range(4)]
        dst_landed, src_landed, attr_landed, nodes_landed = sem("dst_landed"), sem("src_landed"), sem("attr_landed"), sem("nodes_landed")
        ident_made, iota_made, dst_cast, src_cast = sem("ident_made"), sem("iota_made"), sem("dst_cast"), sem("src_cast")
        turned, turn_used = sem("turned"), sem("turn_used")
        step, spans_ready, spans_stored, base_landed = sem("step"), sem("spans_ready"), sem("spans_stored"), sem("base_landed")
        block = ctx.enter_context(nc.Block())

        groups = [(what, k, min(4, TPP - k)) for what in ("src", "dst", "p0", "p1") for k in range(0, TPP, 4)]

        @block.sync
        def _(sp):
            sp.dma_start(dst_i, dst.rearrange("(p f) -> p f", p=PL)).then_inc(dst_landed, 16)
            sp.dma_start(src_i, src.rearrange("(p f) -> p f", p=PL)).then_inc(src_landed, 16)
            sp.dma_start(attr, edge_attr_2.rearrange("(p f) c -> p (f c)", p=PL)).then_inc(attr_landed, 16)
            sp.dma_start(nodes[0:NP, :], x.rearrange("(p j) c -> p (j c)", p=NP)).then_inc(nodes_landed, 16)
            sp.wait_ge(spans_ready, 1)
            sp.dma_start(spans_dram, spans[:, :]).then_inc(spans_stored, 16)
            sp.wait_ge(spans_stored, 16)
            sp.dma_start(base_f[:, :], spans_dram.rearrange("(o b) w -> o (b w)", o=1).to_broadcast([P, B * TW])).then_inc(base_landed, 16)
            sp.wait_ge(nodes_landed, 16)

        @block.gpsimd
        def _(pool):
            pool.memset(ident[:, :], 0.0).then_inc(ident_made, 1)
            pool.wait_ge(ident_made, 1)
            pool.affine_select(out=ident[:, :], in_=ident[:, :], compare_op=ALU.not_equal, fill=1.0, base=0,
                               pattern=[[-1, P]], channel_multiplier=1).then_inc(ident_made, 1)
            pool.iota(keep["iota"][:, :], [[1, WINDOW]], base=0, channel_multiplier=0,
                      allow_small_or_imprecise_dtypes=True).then_inc(iota_made, 1)

        @block.scalar
        def _(act):
            act.wait_ge(src_landed, 16)
            act.activation(src_f, src_i, ACT.Copy).then_inc(src_cast, 1)

        @block.tensor
        def _(pe):
            pe.wait_ge(ident_made, 2)
            for n, (what, k0, width) in enumerate(groups):
                if what == "src":
                    pe.wait_ge(src_cast, 1)
                if what == "dst":
                    pe.wait_ge(dst_cast, 1)
                if what == "p0":
                    pe.wait_ge(attr_landed, 16)
                if n >= 4:
                    pe.wait_ge(turn_used, n - 3)
                for k in range(width):
                    t = k0 + k
                    block_in = {"src": src_f[:, t * P:(t + 1) * P], "dst": dst_f[:, t * P:(t + 1) * P],
                                "p0": attr[:, 2 * t * P:2 * (t + 1) * P:2], "p1": attr[:, 2 * t * P + 1:2 * (t + 1) * P:2]}[what]
                    last = pe.transpose(turn[n % 4][:, k, 0:PL], block_in, ident[0:PL, 0:PL])
                last.then_inc(turned, 1)

        @block.vector
        def _(dve):
            steps = [0]

            def link(ins):
                steps[0] += 1
                ins.then_inc(step, 1)
                dve.wait_ge(step, steps[0])

            dve.wait_ge(dst_landed, 16)
            dve.tensor_copy(dst_f, dst_i).then_inc(dst_cast, 1)
            dve.wait_ge(dst_cast, 1)
            by_tile = dst_f.rearrange("p (t e) -> p t e", e=P)
            dve.tensor_reduce(low[:, :], by_tile, AX_X, ALU.min)
            link(dve.tensor_reduce(high[:, :], by_tile, AX_X, ALU.max))
            dve.memset(spans[:, :], 0.0)
            link(dve.tensor_reduce(span5[:, :], high[:, :].rearrange("p (m t) -> p m t", t=G), AX_X, ALU.max))
            link(dve.tensor_reduce(spans[:, 0:U], low[:, :].rearrange("p (m t) -> p m t", t=G), AX_X, ALU.min))
            link(dve.tensor_tensor(span5[:, :], span5[:, :], spans[:, 0:U], ALU.subtract))
            dve.tensor_reduce(spans[:, U:U + 1], span5[:, :], AX_X, ALU.max).then_inc(spans_ready, 1)

            target = {"src": src_t[:, :], "dst": rel_t[:, :], "p0": pos[:, 0, :], "p1": pos[:, 1, :]}
            for n, (what, k0, width) in enumerate(groups):
                dve.wait_ge(turned, n + 1)
                to = target[what].rearrange("e (p k) -> e k p", k=TPP)[:, k0:k0 + width, :]
                dve.tensor_copy(to, turn[n % 4][:, 0:width, 0:PL]).then_inc(turn_used, 1)
            dve.wait_ge(turn_used, len(groups))

            link(dve.tensor_scalar(pos[:, :, :], pos[:, :, :], 0.0, 1.0, ALU.max, ALU.min))
            link(dve.tensor_scalar(pos[:, :, :], pos[:, :, :], 2.0, -1.0, ALU.mult, ALU.add))
            factors = edge_t[:, :].rearrange("e (t c) -> e t c", c=6)
            for c in range(2):
                dve.tensor_scalar(factors[:, :, 3 * c], pos[:, c, :], -1.0, 0.0, ALU.mult, ALU.max)
                link(dve.tensor_scalar(factors[:, :, 3 * c + 2], pos[:, c, :], 0.0, None, ALU.max))
                link(dve.tensor_tensor(factors[:, :, 3 * c + 1], factors[:, :, 3 * c], factors[:, :, 3 * c + 2], ALU.add))
                link(dve.tensor_scalar(factors[:, :, 3 * c + 1], factors[:, :, 3 * c + 1], -1.0, 1.0, ALU.mult, ALU.add))

            dve.wait_ge(base_landed, 16)
            first = base_f[:, :].rearrange("e (b w) -> e b w", w=TW)
            for m in range(U):
                rel = rel_t[:, :].rearrange("e (b m t) -> e b m t", m=U, t=G)[:, :, m, :]
                dve.tensor_tensor(rel, rel, first[:, :, m:m + 1].to_broadcast([P, B, G]), ALU.subtract)
            link(dve.tensor_reduce(widest[:, :], first[0:1, :, U], AX_X, ALU.max))
            link(dve.tensor_copy(keep["span_i"][:, :], widest[:, :]))


def load_passes(eng, keep):
    return eng.value_load(keep["span_i"][0:1, 0:1], min_val=0, max_val=N - 1) // WINDOW + 1


def start_passes(dve, keep, step, steps):
    dve.tensor_scalar(keep["window"][:, :], keep["iota"][:, :], -float(WINDOW), None, ALU.add)
    dve.tensor_scalar(keep["base_now"][:, :], keep["base_f"][0:1, :], -float(WINDOW), None, ALU.add).then_inc(step, 1)
    dve.wait_ge(step, steps + 1)
    return steps + 1


def next_pass(dve, keep, step, before):
    dve.tensor_scalar(keep["window"][:, :], keep["window"][:, :], float(WINDOW), None, ALU.add)
    dve.tensor_scalar(keep["base_now"][:, :], keep["base_now"][:, :], float(WINDOW), None, ALU.add).then_inc(step, 1)
    dve.wait_ge(step, before + 1)
    dve.tensor_scalar(keep["base_i"][:, :], keep["base_now"][:, :], float(N), None, ALU.min).then_inc(step, 1)
    dve.wait_ge(step, before + 2)


def load_offsets(nc, keep, i):
    row = keep["base_i"][0:1, bass.ds(i * TW, U)]
    _, values = nc.values_load_multi_w_load_instructions(row, engines=(mybir.EngineType.DVE,), min_val=0, max_val=N,
                                                         skip_runtime_bounds_check_because="first destinations are node numbers, and clamped to N")
    return values


def pool_gathers(nc, pool, keep, table, idx, rows, width, idx_ready, gathers_begun, rows_used, rows_landed):
    src_t = keep["src_t"]
    passes = load_passes(pool, keep)

    def gather(g, i, u):
        pool.wait_ge(rows_used, freed(g, u))
        if u in (0, 3):
            n = 3 if u == 0 else 2
            pool.tensor_copy(idx[u // 3][:, 0:n * G], src_t[:, bass.ds(i * (U * G) + u * G, n * G)]).then_inc(idx_ready, 1)
            pool.wait_ge(idx_ready, g * 2 + (1 + u // 3))
        pool.sem_inc(gathers_begun, 1)
        for j in range(G):
            column = (u % 3) * G + j
            pool.indirect_dma_start(out=rows[SLOT[u]][:, j, 0:width], out_offset=None, in_=table,
                                    in_offset=bass.IndirectOffsetOnAxis(ap=idx[u // 3][:, column:column + 1], axis=0)
                                    ).then_inc(rows_landed[SLOT[u]], 16)

    with pool.Fori(0, passes) as p:
        with pool.Fori(0, B) as i:
            g = p * B + i
            for u in range(U):
                gather(g, i, u)


def spline_edges(nc, keep, x, weight0):
    acc, edge_t, rel_t = keep["acc"], keep["edge_t"], keep["rel_t"]
    K = 9 * C
    CH = K // 3
    with ExitStack() as ctx:
        def sbuf(name, shape, dtype=F32):
            return ctx.enter_context(nc.sbuf_tensor(name, shape, dtype))

        def ring(name, shape, dtype=F32):
            return [sbuf(f"{name}{n}", shape, dtype) for n in range(SLOTS)]

        def sem(name):
            return ctx.enter_context(nc.semaphore(name))

        idx = [sbuf("idx_a", [P, 3 * G], I32), sbuf("idx_b", [P, 2 * G], I32)]
        rows = ring("rows", [P, G, C])
        basis = ring("basis", [P, G, 9])
        spread = ring("spread", [P, G, K + 1])
        hot = ring("hot", [P, G, WINDOW])
        sums = ring("sums", [CH + 1, 3 * WINDOW])
        wk = sbuf("wk", [CH + 1, 3, C + 1])
        sums_ps = [ctx.enter_context(nc.psum_tensor(f"sums_ps{n}", [P, 512], F32)) for n in range(SLOTS)]
        msg_ps = [ctx.enter_context(nc.psum_tensor(f"msg_ps{n}", [P, 512], F32)) for n in range(SLOTS)]
        gathers_begun = sem("l0_gathers_begun")
        step, wk_landed, wk_ready, idx_ready = sem("l0_step"), sem("wk_landed"), sem("wk_ready"), sem("l0_idx_ready")
        rows_landed = [sem(f"l0_rows_landed{n}") for n in range(SLOTS)]
        basis_ready, spread_ready, hot_ready = sem("basis_ready"), sem("spread_ready"), sem("l0_hot_ready")
        summed, sums_ready, msg_ready, added = sem("summed"), sem("sums_ready"), sem("l0_msg_ready"), sem("l0_added")
        block = ctx.enter_context(nc.Block())

        @block.sync
        def _(sp):
            sp.wait_ge(wk_ready, 1)
            for c in range(3):
                sp.dma_start(wk[0:CH, c, 0:C], weight0[3 * c:3 * c + 3].rearrange("k i o -> (k i) o")).then_inc(wk_landed, 16)

        @block.gpsimd
        def _(pool):
            pool_gathers(nc, pool, keep, x, idx, rows, C, idx_ready, gathers_begun, spread_ready, rows_landed)

        @block.vector
        def _(dve):
            dve.memset(wk[:, :, :], 0.0).then_inc(wk_ready, 1)
            for n in range(SLOTS):
                dve.memset(spread[n][:, :, K:K + 1], 1.0)
            dve.memset(acc[:, :], 0.0)
            dve.wait_ge(wk_ready, 1)
            dve.memset(wk[CH:CH + 1, 2, C:C + 1], 1.0).then_inc(wk_ready, 1)
            dve.sem_inc(spread_ready, CREDIT)
            steps = start_passes(dve, keep, step, 0)
            passes = load_passes(dve, keep)
            factors = edge_t[:, :].rearrange("e (t c) -> e t c", c=6)

            def build(g, i, u):
                s = SLOT[u]
                tiles = bass.ds(i * (U * G) + u * G, G)
                f = factors[:, tiles, :]
                dve.wait_ge(summed, freed(g, u))
                dve.tensor_tensor(basis[s][:, :, :].rearrange("e t (a b) -> e t a b", b=3),
                                  f[:, :, 0:3].unsqueeze(3).to_broadcast([P, G, 3, 3]),
                                  f[:, :, 3:6].unsqueeze(2).to_broadcast([P, G, 3, 3]), ALU.mult).then_inc(basis_ready, 1)
                dve.tensor_tensor(hot[s][:, :, :], keep["window"][:, :].unsqueeze(1).to_broadcast([P, G, WINDOW]),
                                  rel_t[:, tiles].unsqueeze(2).to_broadcast([P, G, WINDOW]), ALU.is_equal).then_inc(hot_ready, 1)
                dve.wait_ge(basis_ready, done(g, u))
                dve.wait_ge(rows_landed[s], filled(g, u, 16 * G))
                dve.tensor_tensor(spread[s][:, :, 0:K].rearrange("e t (k c) -> e t k c", c=C),
                                  basis[s][:, :, :].unsqueeze(3).to_broadcast([P, G, 9, C]),
                                  rows[s][:, :, :].unsqueeze(2).to_broadcast([P, G, 9, C]), ALU.mult).then_inc(spread_ready, 1)

            def add(g, u, offset):
                dve.wait_ge(msg_ready, done(g, u) + CREDIT)
                dve.wait_ge(added, g * U + (u + CREDIT))
                at = acc[0:C + 1, bass.ds(offset, WINDOW)]
                dve.tensor_tensor(at, at, msg_ps[SLOT[u]][0:C + 1, 0:WINDOW], ALU.add).then_inc(added, 1)

            dve.sem_inc(summed, CREDIT)
            dve.sem_inc(msg_ready, CREDIT)
            dve.sem_inc(added, CREDIT)
            LAG = 2
            with dve.Fori(0, passes) as p:
                next_pass(dve, keep, step, p * 2 + steps)
                for u in range(LAG):
                    build(p * B, 0, u)

                def body(i, last):
                    g = p * B + i
                    offsets = load_offsets(nc, keep, i)
                    for u in range(U):
                        if u + LAG < U:
                            build(g, i, u + LAG)
                        elif not last:
                            build(g + 1, i + 1, u + LAG - U)
                        add(g, u, offsets[u])

                with dve.Fori(0, B - 1) as i:
                    body(i, False)
                body(B - 1, True)

        @block.tensor
        def _(pe):
            pe.wait_ge(wk_landed, 48)
            pe.wait_ge(wk_ready, 2)
            passes = load_passes(pe, keep)

            def sum_edges(g, u):
                s = SLOT[u]
                pe.wait_ge(hot_ready, done(g, u))
                pe.wait_ge(spread_ready, done(g, u) + CREDIT)
                pe.wait_ge(sums_ready, freed(g, u))
                for j in range(G):
                    for c in (2, 0, 1):
                        m = CH + (c == 2)
                        last = pe.matmul(sums_ps[s][0:m, c * WINDOW:(c + 1) * WINDOW], spread[s][:, j, c * CH:c * CH + m],
                                         hot[s][:, j, :], start=(j == 0 and c == 2), stop=(j == G - 1 and c == 1),
                                         skip_group_check=True)
                last.then_inc(summed, 1)

            def weigh(g, u):
                s = SLOT[u]
                pe.wait_ge(sums_ready, done(g, u) + CREDIT)
                pe.wait_ge(added, freed(g, u))
                for c in range(3):
                    m = CH + (c == 2)
                    last = pe.matmul(msg_ps[s][0:C + 1, 0:WINDOW], wk[0:m, c, :], sums[s][0:m, c * WINDOW:(c + 1) * WINDOW],
                                     start=(c == 0), stop=(c == 2))
                last.then_inc(msg_ready, 1)

            with pe.Fori(0, passes) as p:
                sum_edges(p * B, 0)

                def body(i, last):
                    g = p * B + i
                    for u in range(U):
                        if u + 1 < U:
                            sum_edges(g, u + 1)
                        elif not last:
                            sum_edges(g + 1, 0)
                        weigh(g, u)

                with pe.Fori(0, B - 1) as i:
                    body(i, False)
                body(B - 1, True)

        @block.scalar
        def _(act):
            act.sem_inc(sums_ready, CREDIT)
            passes = load_passes(act, keep)
            with act.Fori(0, passes) as p:
                with act.Fori(0, B) as i:
                    g = p * B + i
                    for u in range(U):
                        s = SLOT[u]
                        act.wait_ge(summed, done(g, u) + CREDIT)
                        act.wait_ge(msg_ready, freed(g, u))
                        act.activation(sums[s][0:CH, 0:2 * WINDOW], sums_ps[s][0:CH, 0:2 * WINDOW], ACT.Copy)
                        act.activation(sums[s][0:CH + 1, 2 * WINDOW:3 * WINDOW], sums_ps[s][0:CH + 1, 2 * WINDOW:3 * WINDOW],
                                       ACT.Copy).then_inc(sums_ready, 1)


def inverse_root(dve, value, link, root, approx, half):
    root()
    link(dve.reciprocal(approx, approx))
    link(dve.tensor_tensor(half, approx, approx, ALU.mult))
    link(dve.tensor_tensor(half, half, value, ALU.mult))
    link(dve.tensor_scalar(half, half, -0.5, 1.5, ALU.mult, ALU.add))
    link(dve.tensor_tensor(value, approx, half, ALU.mult))


def normalise(dve, nodes, mean, square, var, tail, link, root):
    t = nodes.rearrange("p (j c) -> p j c", c=C)
    sq = square.rearrange("p (j c) -> p j c", c=C)
    spread = [NP, NJ, C]
    link(dve.tensor_reduce(mean, t, AX_X, ALU.add))
    link(dve.tensor_scalar(mean, mean, 1.0 / C, None, ALU.mult))
    link(dve.tensor_tensor(t, t, mean.unsqueeze(2).to_broadcast(spread), ALU.subtract))
    link(dve.tensor_tensor(sq, t, t, ALU.mult))
    link(dve.tensor_reduce(var, sq, AX_X, ALU.add))
    link(dve.tensor_scalar(var, var, 1.0 / C, EPS, ALU.mult, ALU.add))
    inverse_root(dve, var, link, root, tail, mean)
    link(dve.tensor_tensor(t, t, var.unsqueeze(2).to_broadcast(spread), ALU.mult))


def spline_nodes(nc, keep, root_w, root_b, edge_attr_3, table_dram):
    acc, nodes, ident, edge_t = keep["acc"], keep["nodes"], keep["ident"], keep["edge_t"]
    Q = 4
    groups = NJ // Q
    with ExitStack() as ctx:
        def sbuf(name, shape, dtype=F32):
            return ctx.enter_context(nc.sbuf_tensor(name, shape, dtype))

        def psum(name):
            return ctx.enter_context(nc.psum_tensor(name, [P, 512], F32))

        def sem(name):
            return ctx.enter_context(nc.semaphore(name))

        rw = sbuf("rw", [P, P])
        rws = sbuf("rws", [P, P])
        bias = sbuf("bias", [1, Q, C])
        ones = sbuf("ones", [1, NP])
        turned_x = [sbuf(f"turned_x{n}", [P, NP]) for n in range(2)]
        count = sbuf("count", [NP, 2, Q])
        mean_e = sbuf("mean_e", [NP, 2, Q, C])
        mean, var, rootv = sbuf("mean", [NP, NJ]), sbuf("var", [NP, NJ]), sbuf("rootv", [NP, NJ])
        x_ps = [psum(f"x_ps{n}") for n in range(2)]
        root_ps = [psum(f"root_ps{n}") for n in range(2)]
        agg_ps = [psum(f"agg_ps{n}") for n in range(2)]
        turn_ps = [psum(f"turn_ps{n}") for n in range(2)]
        rws_zero, rw_landed, bias_landed, rw_turned, rw_ready = sem("rws_zero"), sem("rw_landed"), sem("bias_landed"), sem("rw_turned"), sem("rw_ready")
        x_turned, x_copied, root_ready, mixed, step = sem("x_turned"), sem("x_copied"), sem("root_ready"), sem("mixed"), sem("n0_step")
        table_ready, table_stored, acc_free = sem("table_ready"), sem("table_stored"), sem("acc_free")
        rel_landed, rel_turned, rel_used = sem("rel_landed"), sem("rel_turned"), sem("rel_used")
        root_asked, root_taken = sem("root_asked"), sem("root_taken")
        block = ctx.enter_context(nc.Block())
        attr = acc[0:PL, 0:3 * TPP * P]
        table = edge_t[0:NP, 0:NJ * ROW]
        length = edge_t[:, 5 * T:6 * T]
        turns = [(c, k, min(4, TPP - k)) for c in range(3) for k in range(0, TPP, 4)]

        @block.sync
        def _(sp):
            sp.wait_ge(rws_zero, 1)
            for q in range(Q):
                sp.dma_start(rws[q * C:(q + 1) * C, q * C:(q + 1) * C], root_w).then_inc(rw_landed, 16)
                sp.dma_start(bias[:, q, :], root_b.rearrange("(o c) -> o c", o=1)).then_inc(bias_landed, 16)
            sp.wait_ge(mixed, groups)
            sp.dma_start(attr, edge_attr_3.rearrange("(p f) c -> p (f c)", p=PL)).then_inc(rel_landed, 16)
            sp.wait_ge(table_ready, 1)
            sp.dma_start(table_dram.rearrange("(p j) w -> p (j w)", p=NP), table).then_inc(table_stored, 16)
            sp.wait_ge(table_stored, 16)

        @block.tensor
        def _(pe):
            pe.wait_ge(rw_landed, 16 * Q)
            pe.wait_ge(bias_landed, 16 * Q)
            pe.transpose(x_ps[0][:, 0:P], rws[:, :], ident[:, :]).then_inc(rw_turned, 1)
            pe.wait_ge(rw_ready, 2)
            for n in range(groups + 1):
                if n < groups:
                    if n >= 2:
                        pe.wait_ge(x_copied, n - 1)
                    pe.transpose(x_ps[n % 2][:, 0:NP], nodes[0:NP, n * Q * C:(n + 1) * Q * C], ident[0:NP, 0:NP]).then_inc(x_turned, 1)
                if n >= 1:
                    m = n - 1
                    pe.wait_ge(x_copied, m + 1)
                    if m >= 2:
                        pe.wait_ge(mixed, m - 1)
                    pe.matmul(root_ps[m % 2][0:NP, 0:Q * C], turned_x[m % 2][:, :], rw[:, :], start=True, stop=False)
                    pe.matmul(root_ps[m % 2][0:NP, 0:Q * C], ones[:, :], bias[:, :, :].rearrange("o q c -> o (q c)"), start=False, stop=True)
                    for q in range(Q):
                        j = m * Q + q
                        last = pe.matmul(agg_ps[m % 2][0:NP, q * (C + 1):(q + 1) * (C + 1)], acc[0:C + 1, j:j + NJ * (NP - 1) + 1:NJ],
                                         ident[0:C + 1, 0:C + 1], start=True, stop=True)
                    last.then_inc(root_ready, 1)
            pe.wait_ge(rel_landed, 16)
            for n, (c, k0, width) in enumerate(turns):
                if n >= 2:
                    pe.wait_ge(rel_used, n - 1)
                for k in range(width):
                    t = k0 + k
                    last = pe.transpose(turn_ps[n % 2][:, k * P:k * P + PL], attr[:, 3 * t * P + c:3 * (t + 1) * P:3], ident[0:PL, 0:PL])
                last.then_inc(rel_turned, 1)

        @block.scalar
        def _(act):
            act.wait_ge(rw_turned, 1)
            act.activation(rw[:, :], x_ps[0][:, 0:P], ACT.Copy).then_inc(rw_ready, 1)
            for n in range(groups):
                act.wait_ge(x_turned, n + 1)
                if n >= 2:
                    act.wait_ge(root_ready, n - 1)
                act.activation(turned_x[n % 2][:, :], x_ps[n % 2][:, 0:NP], ACT.Copy).then_inc(x_copied, 1)
            for n, (to, what) in enumerate(((rootv[:, :], var[:, :]), (acc[:, 0:T], length))):
                act.wait_ge(root_asked, n + 1)
                act.activation(to, what, ACT.Sqrt).then_inc(root_taken, 1)

        @block.vector
        def _(dve):
            steps = [0]

            def link(ins):
                steps[0] += 1
                ins.then_inc(step, 1)
                dve.wait_ge(step, steps[0])

            dve.memset(rws[:, :], 0.0).then_inc(rws_zero, 1)
            dve.memset(ones[:, :], 1.0).then_inc(rw_ready, 1)
            for n in range(groups):
                b = n % 2
                agg = agg_ps[b][0:NP, 0:Q * (C + 1)].rearrange("p (q c) -> p q c", c=C + 1)
                part = nodes[0:NP, n * Q * C:(n + 1) * Q * C]
                dve.wait_ge(root_ready, n + 1)
                dve.tensor_tensor(part, part, root_ps[b][0:NP, 0:Q * C], ALU.add)
                link(dve.tensor_scalar(count[:, b, :], agg[:, :, C], 1.0, None, ALU.max))
                link(dve.reciprocal(count[:, b, :], count[:, b, :]))
                dve.tensor_tensor(mean_e[:, b, :, :], agg[:, :, 0:C], count[:, b, :].unsqueeze(2).to_broadcast([NP, Q, C]),
                                  ALU.mult).then_inc(mixed, 1)
                dve.wait_ge(mixed, n + 1)
                link(dve.tensor_tensor(part, part, mean_e[:, b, :, :].rearrange("p q c -> p (q c)"), ALU.add))
            roots = [0]

            def root():
                roots[0] += 1
                dve.sem_inc(root_asked, 1)
                dve.wait_ge(root_taken, roots[0])

            normalise(dve, nodes[0:NP, :], mean[:, :], edge_t[0:NP, 0:NJ * C], var[:, :], rootv[:, :], link, root)
            link(dve.memset(table, 0.0))
            rows = table.rearrange("p (j k w) -> p j k w", k=6, w=16)
            t = nodes[0:NP, :].rearrange("p (j c) -> p j c", c=C)
            dve.tensor_copy(rows[:, :, 0, 0:MUL], t[:, :, 0:MUL])
            for k in range(1, 6):
                o = (k - 1) % 3
                last = dve.tensor_copy(rows[:, :, k, 0:MUL], t[:, :, MUL + o:MUL + 3 * MUL:3])
            last.then_inc(table_ready, 1)
            dve.wait_ge(table_stored, 16)
            rho = edge_t[:, 0:5 * T].rearrange("e (t c) -> e t c", c=5)
            for n, (c, k0, width) in enumerate(turns):
                dve.wait_ge(rel_turned, n + 1)
                to = rho[:, :, (c + 2) % 3].rearrange("e (p k) -> e k p", k=TPP)[:, k0:k0 + width, :]
                src_ps = turn_ps[n % 2][:, 0:width * P].rearrange("e (k p) -> e k p", p=P)[:, :, 0:PL]
                dve.tensor_copy(to, src_ps).then_inc(rel_used, 1)
            dve.wait_ge(rel_used, len(turns))
            square = acc[:, 0:3 * T].rearrange("e (t c) -> e t c", c=3)
            link(dve.tensor_tensor(square, rho[:, :, 0:3], rho[:, :, 0:3], ALU.mult))
            link(dve.tensor_reduce(length, square, AX_X, ALU.add))
            inverse_root(dve, length, link, root, acc[:, 0:T], acc[:, T:2 * T])
            link(dve.tensor_tensor(rho[:, :, 0:3], rho[:, :, 0:3], length.unsqueeze(2).to_broadcast([P, T, 3]), ALU.mult))
            link(dve.tensor_copy(rho[:, :, 3:5], rho[:, :, 0:2]))


def tensor_edges(nc, keep, table_dram, edge_weight, w1, b1, w2, b2):
    acc, edge_t, rel_t = keep["acc"], keep["edge_t"], keep["rel_t"]
    c00, c01, c10 = 0.25, 0.25, (3.0 / 32.0) ** 0.5
    k0, k1, k2 = (1.0 / 32.0) ** 0.5, 3.0 ** 0.5 / 8.0, 0.375
    RA = 16 * 16
    PR = RA + 3 * (R - RA)
    OUTS = PR // 16
    X, Y = 3, G - 3
    with ExitStack() as ctx:
        def sbuf(name, shape, dtype=F32):
            return ctx.enter_context(nc.sbuf_tensor(name, shape, dtype))

        def ring(name, shape, dtype=F32):
            return [sbuf(f"{name}{n}", shape, dtype) for n in range(SLOTS)]

        def psum(name, shape):
            return ctx.enter_context(nc.psum_tensor(name, shape, F32))

        def sem(name):
            return ctx.enter_context(nc.semaphore(name))

        idx = [sbuf("idx1_a", [P, 3 * G], I32), sbuf("idx1_b", [P, 2 * G], I32)]
        rows = ring("rows1", [P, G, ROW])
        dist = ring("dist", [HID, G * P])
        hidden = ring("hidden", [P, G * P])
        hot = ring("hot1", [P, G, WINDOW])
        dots = sbuf("dots", [P, G, 3, MUL])
        turn_a = sbuf("turn_a", [P, G, 3, MUL])
        turn_b = sbuf("turn_b", [P, G, 3, MUL])
        spare = edge_t[:, 5 * T:6 * T]
        prods = [spare[:, 0:X * PR].rearrange("e (t c) -> e t c", c=PR), sbuf("prods_y", [P, Y, PR])[:, :, :]]
        w2p = spare[:, X * PR:X * PR + R]
        w2raw = spare[0:HID + 1, X * PR + R:X * PR + 2 * R]
        outs = ring("outs", [P, G, OUTS])
        along = sbuf("along", [P, G, MUL, 3])
        w1c, b1c = sbuf("w1c", [HID, 1]), sbuf("b1c", [HID, 1])
        radial = [psum("radial_x", [P, X, 512]), psum("radial_y", [P, Y, 512])]
        msg_ps = [psum(f"msg1_ps{n}", [P, 512]) for n in range(SLOTS)]
        gathers_begun = sem("l1_gathers_begun")
        step, idx_ready, w_landed, w_zero, w_ready = sem("l1_step"), sem("l1_idx_ready"), sem("w_landed"), sem("w_zero"), sem("w_ready")
        rows_landed = [sem(f"l1_rows_landed{n}") for n in range(SLOTS)]
        dist_landed = [sem(f"dist_landed{n}") for n in range(SLOTS)]
        hidden_ready, hot_ready = sem("hidden_ready"), sem("l1_hot_ready")
        dots_ready, turns_ready, inputs_ready = sem("dots_ready"), sem("turns_ready"), sem("inputs_ready")
        radial_ready = [sem("radial_x_ready"), sem("radial_y_ready")]
        prods_ready = [sem("prods_x_ready"), sem("prods_y_ready")]
        outs_ready, along_ready, vectors_ready, msg_ready, added = sem("outs_ready"), sem("along_ready"), sem("vectors_ready"), sem("l1_msg_ready"), sem("l1_added")
        block = ctx.enter_context(nc.Block())

        @block.sync
        def _(sp):
            sp.dma_start(w2raw[0:HID, :], w2).then_inc(w_landed, 16)
            sp.dma_start(w2raw[HID:HID + 1, :], b2.rearrange("(o r) -> o r", o=1)).then_inc(w_landed, 16)
            sp.dma_start(w1c[:, :], w1.rearrange("o h -> h o")).then_inc(w_landed, 16)
            sp.dma_start(b1c[:, :], b1.rearrange("(h o) -> h o", o=1)).then_inc(w_landed, 16)
            passes = load_passes(sp, keep)
            with sp.Fori(0, passes) as p:
                with sp.Fori(0, B) as i:
                    g = p * B + i
                    for u in range(U):
                        sp.wait_ge(hidden_ready, freed(g, u))
                        part = edge_weight[bass.ds(i * (U * G * P) + u * G * P, G * P)]
                        sp.dma_start(dist[SLOT[u]][:, :], part.rearrange("(o e) -> o e", o=1).to_broadcast([HID, G * P])
                                     ).then_inc(dist_landed[SLOT[u]], 16)

        @block.gpsimd
        def _(pool):
            pool_gathers(nc, pool, keep, table_dram, idx, rows, ROW, idx_ready, gathers_begun, prods_ready[1], rows_landed)

        @block.scalar
        def _(act):
            act.wait_ge(w_landed, 64)
            act.sem_inc(hidden_ready, CREDIT)
            passes = load_passes(act, keep)
            with act.Fori(0, passes) as p:
                with act.Fori(0, B) as i:
                    g = p * B + i
                    for u in range(U):
                        s = SLOT[u]
                        act.wait_ge(dist_landed[s], filled(g, u, 16))
                        act.wait_ge(radial_ready[1], freed(g, u))
                        act.activation(hidden[s][0:HID, :], dist[s][:, :], ACT.Relu, bias=b1c[:, 0:1], scale=w1c[:, 0:1]
                                       ).then_inc(hidden_ready, 1)

        @block.tensor
        def _(pe):
            pe.wait_ge(w_ready, 1)
            pe.sem_inc(radial_ready[1], CREDIT)
            passes = load_passes(pe, keep)

            def radials(g, u):
                s = SLOT[u]
                pe.wait_ge(hidden_ready, done(g, u) + CREDIT)
                for h, (j0, tiles) in enumerate(((0, X), (X, Y))):
                    pe.wait_ge(prods_ready[h], g * U + (u + CREDIT))
                    for j in range(tiles):
                        last = pe.matmul(radial[h][:, j, 0:R], hidden[s][:, (j0 + j) * P:(j0 + j + 1) * P], w2p[:, :],
                                         start=True, stop=True)
                    last.then_inc(radial_ready[h], 1)

            def sum_edges(g, u):
                s = SLOT[u]
                pe.wait_ge(vectors_ready, done(g, u))
                pe.wait_ge(hot_ready, done(g, u))
                pe.wait_ge(added, freed(g, u))
                for j in range(G):
                    last = pe.matmul(msg_ps[s][0:C, 0:WINDOW], outs[s][:, j, MUL:OUTS], hot[s][:, j, :], start=(j == 0), stop=(j == G - 1))
                last.then_inc(msg_ready, 1)

            with pe.Fori(0, passes) as p:
                radials(p * B, 0)

                def body(i, last):
                    g = p * B + i
                    for u in range(U):
                        if u + 1 < U:
                            radials(g, u + 1)
                        elif not last:
                            radials(g + 1, 0)
                        sum_edges(g, u)

                with pe.Fori(0, B - 1) as i:
                    body(i, False)
                body(B - 1, True)

        @block.vector
        def _(dve):
            for n in range(SLOTS):
                dve.memset(hidden[n][HID:P, :], 0.0).then_inc(w_zero, 1)
            dve.memset(w2p[:, :], 0.0).then_inc(w_zero, 1)
            dve.memset(acc[:, :], 0.0)
            dve.wait_ge(w_zero, SLOTS + 1)
            for n in range(SLOTS):
                dve.memset(hidden[n][HID:HID + 1, :], 1.0)
            dve.wait_ge(w_landed, 64)
            K = HID + 1
            mul2 = lambda lo: w2raw[:, lo:lo + 64].rearrange("h (u v) -> h u v", v=MUL)
            r11 = w2raw[:, 192:R].rearrange("h (u v k) -> h u v k", v=MUL, k=3)
            pa = w2p[0:K, 0:RA].rearrange("h (o i) -> h o i", i=16)
            pb = w2p[0:K, RA:R].rearrange("h (o i) -> h o i", i=16)
            dve.tensor_scalar(pa[:, MUL:16, 0:MUL], mul2(0), c00, None, ALU.mult)
            dve.tensor_scalar(pa[:, MUL:16, MUL:16], mul2(64), c01, None, ALU.mult)
            dve.tensor_scalar(pa[:, 0:MUL, 0:MUL], mul2(128), c10, None, ALU.mult)
            dve.tensor_scalar(pa[:, 0:MUL, MUL:16], r11[:, :, :, 2], k2, None, ALU.mult)
            dve.tensor_scalar(pb[:, :, MUL:16], r11[:, :, :, 1], k1, None, ALU.mult)
            dve.tensor_scalar(pb[:, :, 0:MUL], r11[:, :, :, 2], -k2 / 3.0, None, ALU.mult).then_inc(w_zero, 1)
            dve.wait_ge(w_zero, SLOTS + 2)
            dve.scalar_tensor_tensor(out=pb[:, :, 0:MUL], in0=r11[:, :, :, 0], scalar=k0, in1=pb[:, :, 0:MUL], op0=ALU.mult,
                                     op1=ALU.add).then_inc(w_ready, 1)
            dve.sem_inc(added, CREDIT)
            for h in range(2):
                dve.sem_inc(prods_ready[h], CREDIT)
            steps = start_passes(dve, keep, step, 0)
            passes = load_passes(dve, keep)
            rho_t = edge_t[:, 0:5 * T].rearrange("e (t c) -> e t c", c=5)
            VEC = [P, G, 3, MUL]

            def inputs_a(g, i, u):
                s = SLOT[u]
                tiles = bass.ds(i * (U * G) + u * G, G)
                rho = rho_t[:, tiles, :]
                comp = rows[s][:, :, :].rearrange("e t (k w) -> e t k w", w=16)
                dve.wait_ge(rows_landed[s], filled(g, u, 16 * G))
                dve.tensor_tensor(dots[:, :, :, :], comp[:, :, 1:4, 0:MUL], rho[:, :, 0:3].unsqueeze(3).to_broadcast(VEC), ALU.mult
                                  ).then_inc(dots_ready, 1)
                dve.tensor_tensor(turn_a[:, :, :, :], comp[:, :, 3:6, 0:MUL], rho[:, :, 1:4].unsqueeze(3).to_broadcast(VEC), ALU.mult)
                dve.tensor_tensor(turn_b[:, :, :, :], comp[:, :, 2:5, 0:MUL], rho[:, :, 2:5].unsqueeze(3).to_broadcast(VEC), ALU.mult
                                  ).then_inc(turns_ready, 1)
                dve.wait_ge(msg_ready, freed(g, u))
                dve.tensor_tensor(hot[s][:, :, :], keep["window"][:, :].unsqueeze(1).to_broadcast([P, G, WINDOW]),
                                  rel_t[:, tiles].unsqueeze(2).to_broadcast([P, G, WINDOW]), ALU.is_equal).then_inc(hot_ready, 1)

            def inputs_b(g, u):
                s = SLOT[u]
                comp = rows[s][:, :, :].rearrange("e t (k w) -> e t k w", w=16)
                dve.wait_ge(dots_ready, done(g, u))
                dve.tensor_reduce(comp[:, :, 0, MUL:16], dots[:, :, :, :].rearrange("e t o v -> e t v o"), AX_X, ALU.add)
                dve.wait_ge(turns_ready, done(g, u))
                dve.tensor_tensor(comp[:, :, 1:4, MUL:16], turn_a[:, :, :, :], turn_b[:, :, :, :], ALU.subtract).then_inc(inputs_ready, 1)

            def products(g, u, h):
                s = SLOT[u]
                j0, tiles = ((0, X), (X, Y))[h]
                if h == 0:
                    dve.wait_ge(inputs_ready, done(g, u))
                dve.wait_ge(radial_ready[h], done(g, u) + (CREDIT if h else 0))
                comp = rows[s][:, j0:j0 + tiles, :].rearrange("e t (k w) -> e t k w", w=16)
                ra = radial[h][:, :, 0:RA].rearrange("e t (o i) -> e t o i", i=16)
                dve.tensor_tensor(prods[h][:, :, 0:RA].rearrange("e t (o i) -> e t o i", i=16), ra,
                                  comp[:, :, 0:1, :].to_broadcast([P, tiles, 16, 16]), ALU.mult)
                for j in range(tiles):
                    rb = radial[h][:, j, RA:R].rearrange("e (u i) -> e u i", i=16).unsqueeze(2).to_broadcast([P, MUL, 3, 16])
                    last = dve.tensor_tensor(prods[h][:, j, RA:PR].rearrange("e (u o i) -> e u o i", o=3, i=16), rb,
                                             comp[:, j, 1:4, :].unsqueeze(1).to_broadcast([P, MUL, 3, 16]), ALU.mult)
                last.then_inc(prods_ready[h], 1)

            def reduce(g, u, h):
                s = SLOT[u]
                j0, tiles = ((0, X), (X, Y))[h]
                dve.wait_ge(prods_ready[h], done(g, u) + CREDIT)
                dve.tensor_reduce(outs[s][:, j0:j0 + tiles, :], prods[h][:, :, :].rearrange("e t (o i) -> e t o i", i=16), AX_X, ALU.add
                                  ).then_inc(outs_ready, 1)

            def vectors_a(g, i, u):
                s = SLOT[u]
                rho = rho_t[:, bass.ds(i * (U * G) + u * G, G), 0:3]
                dve.wait_ge(outs_ready, g * (2 * U) + 2 * (u + 1))
                dve.tensor_tensor(along[:, :, :, :], outs[s][:, :, 0:MUL].unsqueeze(3).to_broadcast([P, G, MUL, 3]),
                                  rho.unsqueeze(2).to_broadcast([P, G, MUL, 3]), ALU.mult).then_inc(along_ready, 1)

            def vectors_b(g, u):
                s = SLOT[u]
                dve.wait_ge(along_ready, done(g, u))
                vec = outs[s][:, :, 2 * MUL:OUTS]
                dve.tensor_tensor(vec, vec, along[:, :, :, :].rearrange("e t u o -> e t (u o)"), ALU.add).then_inc(vectors_ready, 1)

            def add(g, u, offset):
                dve.wait_ge(msg_ready, done(g, u) + CREDIT)
                dve.wait_ge(added, g * U + (u + CREDIT))
                at = acc[0:C, bass.ds(offset, WINDOW)]
                dve.tensor_tensor(at, at, msg_ps[SLOT[u]][0:C, 0:WINDOW], ALU.add).then_inc(added, 1)

            dve.sem_inc(msg_ready, CREDIT)
            with dve.Fori(0, passes) as p:
                next_pass(dve, keep, step, p * 2 + steps)
                inputs_a(p * B, 0, 0)
                inputs_b(p * B, 0)

                def body(i, last):
                    g = p * B + i
                    offsets = load_offsets(nc, keep, i)
                    for u in range(U):
                        if not last or u + 1 < U:
                            gn, un = place(g, u + 1)
                            i_n = place(i, u + 1)[0]
                            ahead = True
                        else:
                            ahead = False
                        products(g, u, 0)
                        if ahead:
                            inputs_a(gn, i_n, un)
                        reduce(g, u, 0)
                        products(g, u, 1)
                        if ahead:
                            inputs_b(gn, un)
                        reduce(g, u, 1)
                        vectors_a(g, i, u)
                        if u:
                            add(g, u - 1, offsets[u - 1])
                        vectors_b(g, u)
                    add(g, U - 1, offsets[U - 1])

                with dve.Fori(0, B - 1) as i:
                    body(i, False)
                body(B - 1, True)


def tensor_nodes(nc, keep, out):
    acc, nodes, ident, edge_t = keep["acc"], keep["nodes"], keep["ident"], keep["edge_t"]
    Q = 10
    groups = NJ // Q
    with ExitStack() as ctx:
        def sem(name):
            return ctx.enter_context(nc.semaphore(name))

        agg_ps = [ctx.enter_context(nc.psum_tensor(f"agg1_ps{n}", [P, 512], F32)) for n in range(2)]
        mean = ctx.enter_context(nc.sbuf_tensor("mean1", [NP, NJ], F32))
        var = ctx.enter_context(nc.sbuf_tensor("var1", [NP, NJ], F32))
        rootv = ctx.enter_context(nc.sbuf_tensor("rootv1", [NP, NJ], F32))
        turned, mixed, step, result, stored = sem("n1_turned"), sem("n1_mixed"), sem("n1_step"), sem("result"), sem("stored")
        root_asked, root_taken = sem("n1_root_asked"), sem("n1_root_taken")
        block = ctx.enter_context(nc.Block())

        @block.tensor
        def _(pe):
            for n in range(groups):
                if n >= 2:
                    pe.wait_ge(mixed, n - 1)
                for q in range(Q):
                    j = n * Q + q
                    last = pe.matmul(agg_ps[n % 2][0:NP, q * C:(q + 1) * C], acc[0:C, j:j + NJ * (NP - 1) + 1:NJ], ident[0:C, 0:C],
                                     start=True, stop=True)
                last.then_inc(turned, 1)

        @block.vector
        def _(dve):
            steps = [0]

            def link(ins):
                steps[0] += 1
                ins.then_inc(step, 1)
                dve.wait_ge(step, steps[0])

            for n in range(groups):
                part = nodes[0:NP, n * Q * C:(n + 1) * Q * C]
                dve.wait_ge(turned, n + 1)
                dve.tensor_tensor(part, part, agg_ps[n % 2][0:NP, 0:Q * C], ALU.add).then_inc(mixed, 1)
            dve.wait_ge(mixed, groups)
            def root():
                dve.sem_inc(root_asked, 1)
                dve.wait_ge(root_taken, 1)

            normalise(dve, nodes[0:NP, :], mean[:, :], edge_t[0:NP, 0:NJ * C], var[:, :], rootv[:, :], link, root)
            dve.sem_inc(result, 1)

        @block.scalar
        def _(act):
            act.wait_ge(root_asked, 1)
            act.activation(rootv[:, :], var[:, :], ACT.Sqrt).then_inc(root_taken, 1)

        @block.sync
        def _(sp):
            sp.wait_ge(result, 1)
            sp.dma_start(out.rearrange("(p j) c -> p (j c)", p=NP), nodes[0:NP, :]).then_inc(stored, 16)
            sp.wait_ge(stored, 16)


_INS = ["x", "src", "dst", "edge_attr_2", "edge_attr_3", "edge_weight", "L0_gnn_weight", "L0_gnn_root_w", "L0_gnn_root_b",
        "L1_gnn_w1", "L1_gnn_b1", "L1_gnn_w2", "L1_gnn_b2"]


def kernel(**inputs):
    import numpy as _np
    import concourse.bacc as _bacc
    from concourse import mybir as _mybir
    from concourse.bass_utils import run_bass_kernel_spmd as _run

    nc = _bacc.Bacc("TRN2", target_bir_lowering=False, num_devices=1)
    arrays, args = {}, []
    for name in _INS:
        a = _np.ascontiguousarray(inputs[name])
        arrays[f"in_{name}"] = a
        args.append(nc.dram_tensor(f"in_{name}", a.shape, _mybir.dt.from_np(a.dtype), kind="ExternalInput").ap())
    result = nc.dram_tensor("out", (N, C), _mybir.dt.float32, kind="ExternalOutput").ap()
    build_program(nc, *args, result)
    r = _run(nc, [arrays], core_ids=[0])
    return r.results[0]["out"]
```
